# Optimizing a Trainium2 kernel written in Bass

```python
import numpy as np
import jax
import jax.numpy as jnp

def _softmax(x, axis=-1):
    return jax.nn.softmax(x, axis=axis)

def _gelu(x):
    return jax.nn.gelu(x, approximate=True)

def _silu(x):
    return jax.nn.silu(x)

def _sigmoid(x):
    return jax.nn.sigmoid(x)

def _layernorm(x, axis=-1, eps=1e-05):
    m = jnp.mean(x, axis=axis, keepdims=True)
    v = jnp.var(x, axis=axis, keepdims=True)
    return (x - m) / jnp.sqrt(v + eps)

def _scatter_add(tgt, idx, src, axis=0):
    return tgt.at[idx].add(src)

def _segment_sum(src, seg, n):
    return jax.ops.segment_sum(src, seg, n)
kernel_name = 'mk_dlrm_tower_d1_rec_r8_920403'

def setup_inputs(seed: int=0):
    np.random.seed(seed)
    _w = jnp.asarray

    def _rec_inputs():
        import jax
        import jax.numpy as jnp
        _tk = jax.random.key(seed)
        dense_ctx = jax.random.normal(jax.random.fold_in(_tk, 190), (1024, 16), jnp.float32)
        ids = jnp.stack([jax.random.randint(jax.random.fold_in(_tk, 200 + f), (1024,), 0, v, jnp.int32) for f, v in enumerate([1000, 1250, 1000, 1250, 1000, 1250, 12500, 1000, 12500, 12500, 12500, 125000, 1250, 1000, 12500, 125000, 1250, 1250, 125000, 12500, 125000, 125000, 12500, 12500, 1250, 1000, 125000, 12500, 12500, 12500, 1000, 1250, 1000, 1000, 12500, 1250, 12500, 1250, 12500])], axis=1)
        tbl_0 = 0.05 * jax.random.normal(jax.random.fold_in(_tk, 500 + 0), (1000, 32), jnp.float32)
        tbl_1 = 0.05 * jax.random.normal(jax.random.fold_in(_tk, 500 + 1), (1250, 32), jnp.float32)
        tbl_2 = 0.05 * jax.random.normal(jax.random.fold_in(_tk, 500 + 2), (1000, 32), jnp.float32)
        tbl_3 = 0.05 * jax.random.normal(jax.random.fold_in(_tk, 500 + 3), (1250, 32), jnp.float32)
        tbl_4 = 0.05 * jax.random.normal(jax.random.fold_in(_tk, 500 + 4), (1000, 32), jnp.float32)
        tbl_5 = 0.05 * jax.random.normal(jax.random.fold_in(_tk, 500 + 5), (1250, 32), jnp.float32)
        tbl_6 = 0.05 * jax.random.normal(jax.random.fold_in(_tk, 500 + 6), (12500, 32), jnp.float32)
        tbl_7 = 0.05 * jax.random.normal(jax.random.fold_in(_tk, 500 + 7), (1000, 32), jnp.float32)
        tbl_8 = 0.05 * jax.random.normal(jax.random.fold_in(_tk, 500 + 8), (12500, 32), jnp.float32)
        tbl_9 = 0.05 * jax.random.normal(jax.random.fold_in(_tk, 500 + 9), (12500, 32), jnp.float32)
        tbl_10 = 0.05 * jax.random.normal(jax.random.fold_in(_tk, 500 + 10), (12500, 32), jnp.float32)
        tbl_11 = 0.05 * jax.random.normal(jax.random.fold_in(_tk, 500 + 11), (125000, 32), jnp.float32)
        tbl_12 = 0.05 * jax.random.normal(jax.random.fold_in(_tk, 500 + 12), (1250, 32), jnp.float32)
        tbl_13 = 0.05 * jax.random.normal(jax.random.fold_in(_tk, 500 + 13), (1000, 32), jnp.float32)
        tbl_14 = 0.05 * jax.random.normal(jax.random.fold_in(_tk, 500 + 14), (12500, 32), jnp.float32)
        tbl_15 = 0.05 * jax.random.normal(jax.random.fold_in(_tk, 500 + 15), (125000, 32), jnp.float32)
        tbl_16 = 0.05 * jax.random.normal(jax.random.fold_in(_tk, 500 + 16), (1250, 32), jnp.float32)
        tbl_17 = 0.05 * jax.random.normal(jax.random.fold_in(_tk, 500 + 17), (1250, 32), jnp.float32)
        tbl_18 = 0.05 * jax.random.normal(jax.random.fold_in(_tk, 500 + 18), (125000, 32), jnp.float32)
        tbl_19 = 0.05 * jax.random.normal(jax.random.fold_in(_tk, 500 + 19), (12500, 32), jnp.float32)
        tbl_20 = 0.05 * jax.random.normal(jax.random.fold_in(_tk, 500 + 20), (125000, 32), jnp.float32)
        tbl_21 = 0.05 * jax.random.normal(jax.random.fold_in(_tk, 500 + 21), (125000, 32), jnp.float32)
        tbl_22 = 0.05 * jax.random.normal(jax.random.fold_in(_tk, 500 + 22), (12500, 32), jnp.float32)
        tbl_23 = 0.05 * jax.random.normal(jax.random.fold_in(_tk, 500 + 23), (12500, 32), jnp.float32)
        tbl_24 = 0.05 * jax.random.normal(jax.random.fold_in(_tk, 500 + 24), (1250, 32), jnp.float32)
        tbl_25 = 0.05 * jax.random.normal(jax.random.fold_in(_tk, 500 + 25), (1000, 32), jnp.float32)
        tbl_26 = 0.05 * jax.random.normal(jax.random.fold_in(_tk, 500 + 26), (125000, 32), jnp.float32)
        tbl_27 = 0.05 * jax.random.normal(jax.random.fold_in(_tk, 500 + 27), (12500, 32), jnp.float32)
        tbl_28 = 0.05 * jax.random.normal(jax.random.fold_in(_tk, 500 + 28), (12500, 32), jnp.float32)
        tbl_29 = 0.05 * jax.random.normal(jax.random.fold_in(_tk, 500 + 29), (12500, 32), jnp.float32)
        tbl_30 = 0.05 * jax.random.normal(jax.random.fold_in(_tk, 500 + 30), (1000, 32), jnp.float32)
        tbl_31 = 0.05 * jax.random.normal(jax.random.fold_in(_tk, 500 + 31), (1250, 32), jnp.float32)
        tbl_32 = 0.05 * jax.random.normal(jax.random.fold_in(_tk, 500 + 32), (1000, 32), jnp.float32)
        tbl_33 = 0.05 * jax.random.normal(jax.random.fold_in(_tk, 500 + 33), (1000, 32), jnp.float32)
        tbl_34 = 0.05 * jax.random.normal(jax.random.fold_in(_tk, 500 + 34), (12500, 32), jnp.float32)
        tbl_35 = 0.05 * jax.random.normal(jax.random.fold_in(_tk, 500 + 35), (1250, 32), jnp.float32)
        tbl_36 = 0.05 * jax.random.normal(jax.random.fold_in(_tk, 500 + 36), (12500, 32), jnp.float32)
        tbl_37 = 0.05 * jax.random.normal(jax.random.fold_in(_tk, 500 + 37), (1250, 32), jnp.float32)
        tbl_38 = 0.05 * jax.random.normal(jax.random.fold_in(_tk, 500 + 38), (12500, 32), jnp.float32)
        _rk = jax.random.fold_in(_tk, 7)
        W_top1 = 0.0693375 * jax.random.normal(jax.random.fold_in(_tk, 801), (208, 512), jnp.float32)
        W_top2 = 0.0441942 * jax.random.normal(jax.random.fold_in(_tk, 802), (512, 256), jnp.float32)
        W_top3 = 0.0625 * jax.random.normal(jax.random.fold_in(_tk, 803), (256, 1), jnp.float32)
        b_top1 = jnp.zeros((512,), jnp.float32)
        b_top2 = jnp.zeros((256,), jnp.float32)
        return (dense_ctx, ids, tbl_0, tbl_1, tbl_2, tbl_3, tbl_4, tbl_5, tbl_6, tbl_7, tbl_8, tbl_9, tbl_10, tbl_11, tbl_12, tbl_13, tbl_14, tbl_15, tbl_16, tbl_17, tbl_18, tbl_19, tbl_20, tbl_21, tbl_22, tbl_23, tbl_24, tbl_25, tbl_26, tbl_27, tbl_28, tbl_29, tbl_30, tbl_31, tbl_32, tbl_33, tbl_34, tbl_35, tbl_36, tbl_37, tbl_38, W_top1, b_top1, W_top2, b_top2, W_top3)
    dense_ctx, ids, tbl_0, tbl_1, tbl_2, tbl_3, tbl_4, tbl_5, tbl_6, tbl_7, tbl_8, tbl_9, tbl_10, tbl_11, tbl_12, tbl_13, tbl_14, tbl_15, tbl_16, tbl_17, tbl_18, tbl_19, tbl_20, tbl_21, tbl_22, tbl_23, tbl_24, tbl_25, tbl_26, tbl_27, tbl_28, tbl_29, tbl_30, tbl_31, tbl_32, tbl_33, tbl_34, tbl_35, tbl_36, tbl_37, tbl_38, W_top1, b_top1, W_top2, b_top2, W_top3 = _rec_inputs()

    def _L0_rec_setup():
        import jax, jax.numpy as jnp
        import numpy as np
        LAYER_SIZES = (128, 128)

        def _cin_layer(h0, h, W):
            F0, Fi = (h0.shape[1], h.shape[1])
            K = W.shape[1]
            Wr = W.reshape(F0, Fi, K)
            return jnp.einsum('bid,bjd,ijk->bkd', h0, h, Wr)
        key = jax.random.key(seed)
        k1, k2, k3 = jax.random.split(key, 3)
        B, F0, D = (256, 39, 32)
        F1 = LAYER_SIZES[0] // 2
        x = jax.random.normal(k1, (B, F0, D), dtype=jnp.float32)
        W1 = jax.random.normal(k2, (F0 * F0, LAYER_SIZES[0]), dtype=jnp.float32) * 0.05
        W2 = jax.random.normal(k3, (F0 * F1, LAYER_SIZES[1]), dtype=jnp.float32) * 0.05
        return {'x': x, 'W1': W1, 'W2': W2}
    _L0_rec_all = _L0_rec_setup()
    _L0_rec_in = {k: v for k, v in _L0_rec_all.items() if k in ('W1', 'W2')}
    del _L0_rec_all
    return {'dense_ctx': dense_ctx, 'ids': ids, 'tbl_0': tbl_0, 'tbl_1': tbl_1, 'tbl_2': tbl_2, 'tbl_3': tbl_3, 'tbl_4': tbl_4, 'tbl_5': tbl_5, 'tbl_6': tbl_6, 'tbl_7': tbl_7, 'tbl_8': tbl_8, 'tbl_9': tbl_9, 'tbl_10': tbl_10, 'tbl_11': tbl_11, 'tbl_12': tbl_12, 'tbl_13': tbl_13, 'tbl_14': tbl_14, 'tbl_15': tbl_15, 'tbl_16': tbl_16, 'tbl_17': tbl_17, 'tbl_18': tbl_18, 'tbl_19': tbl_19, 'tbl_20': tbl_20, 'tbl_21': tbl_21, 'tbl_22': tbl_22, 'tbl_23': tbl_23, 'tbl_24': tbl_24, 'tbl_25': tbl_25, 'tbl_26': tbl_26, 'tbl_27': tbl_27, 'tbl_28': tbl_28, 'tbl_29': tbl_29, 'tbl_30': tbl_30, 'tbl_31': tbl_31, 'tbl_32': tbl_32, 'tbl_33': tbl_33, 'tbl_34': tbl_34, 'tbl_35': tbl_35, 'tbl_36': tbl_36, 'tbl_37': tbl_37, 'tbl_38': tbl_38, 'W_top1': W_top1, 'b_top1': b_top1, 'W_top2': W_top2, 'b_top2': b_top2, 'W_top3': W_top3, 'L0_rec_W1': _L0_rec_in['W1'], 'L0_rec_W2': _L0_rec_in['W2']}

def reference(dense_ctx, ids, tbl_0, tbl_1, tbl_2, tbl_3, tbl_4, tbl_5, tbl_6, tbl_7, tbl_8, tbl_9, tbl_10, tbl_11, tbl_12, tbl_13, tbl_14, tbl_15, tbl_16, tbl_17, tbl_18, tbl_19, tbl_20, tbl_21, tbl_22, tbl_23, tbl_24, tbl_25, tbl_26, tbl_27, tbl_28, tbl_29, tbl_30, tbl_31, tbl_32, tbl_33, tbl_34, tbl_35, tbl_36, tbl_37, tbl_38, W_top1, b_top1, W_top2, b_top2, W_top3, L0_rec_W1, L0_rec_W2):
    import jax
    import jax.numpy as jnp

    def _L0_rec_ref(x, W1, W2):
        import jax, jax.numpy as jnp
        import numpy as np
        LAYER_SIZES = (128, 128)

        def _cin_layer(h0, h, W):
            F0, Fi = (h0.shape[1], h.shape[1])
            K = W.shape[1]
            Wr = W.reshape(F0, Fi, K)
            return jnp.einsum('bid,bjd,ijk->bkd', h0, h, Wr)
        conv1 = _cin_layer(x, x, W1)
        half = LAYER_SIZES[0] // 2
        hidden1 = conv1[:, :half, :]
        final1 = conv1[:, half:, :]
        conv2 = _cin_layer(x, hidden1, W2)
        final = jnp.concatenate([final1, conv2], axis=1)
        return jnp.sum(final, axis=2)
    e = jnp.stack([tbl_0[ids[:, 0]], tbl_1[ids[:, 1]], tbl_2[ids[:, 2]], tbl_3[ids[:, 3]], tbl_4[ids[:, 4]], tbl_5[ids[:, 5]], tbl_6[ids[:, 6]], tbl_7[ids[:, 7]], tbl_8[ids[:, 8]], tbl_9[ids[:, 9]], tbl_10[ids[:, 10]], tbl_11[ids[:, 11]], tbl_12[ids[:, 12]], tbl_13[ids[:, 13]], tbl_14[ids[:, 14]], tbl_15[ids[:, 15]], tbl_16[ids[:, 16]], tbl_17[ids[:, 17]], tbl_18[ids[:, 18]], tbl_19[ids[:, 19]], tbl_20[ids[:, 20]], tbl_21[ids[:, 21]], tbl_22[ids[:, 22]], tbl_23[ids[:, 23]], tbl_24[ids[:, 24]], tbl_25[ids[:, 25]], tbl_26[ids[:, 26]], tbl_27[ids[:, 27]], tbl_28[ids[:, 28]], tbl_29[ids[:, 29]], tbl_30[ids[:, 30]], tbl_31[ids[:, 31]], tbl_32[ids[:, 32]], tbl_33[ids[:, 33]], tbl_34[ids[:, 34]], tbl_35[ids[:, 35]], tbl_36[ids[:, 36]], tbl_37[ids[:, 37]], tbl_38[ids[:, 38]]], axis=1)
    z = _L0_rec_ref(e, L0_rec_W1, L0_rec_W2)
    z = z.reshape(z.shape[0], -1)
    h = jnp.concatenate([z, dense_ctx], axis=1)
    h = jnp.maximum(h @ W_top1 + b_top1, 0.0)
    h = jnp.maximum(h @ W_top2 + b_top2, 0.0)
    y = h @ W_top3
    return y

_drawn_inputs = setup_inputs


def setup_inputs(seed=0):
    import zlib

    import numpy as np

    out = dict(_drawn_inputs(seed))
    spreads = {'b_top1': (0.0, 0.1), 'b_top2': (0.0, 0.1)}
    factors = {'tbl_0': 4.72,
     'tbl_1': 4.817,
     'tbl_2': 5.017,
     'tbl_3': 5.077,
     'tbl_4': 4.972,
     'tbl_5': 4.535,
     'tbl_6': 4.74,
     'tbl_7': 4.555,
     'tbl_8': 4.862,
     'tbl_9': 4.891,
     'tbl_10': 5.114,
     'tbl_11': 4.502,
     'tbl_12': 4.843,
     'tbl_13': 4.784,
     'tbl_14': 4.585,
     'tbl_15': 4.842,
     'tbl_16': 4.228,
     'tbl_17': 4.638,
     'tbl_18': 4.751,
     'tbl_19': 4.992,
     'tbl_20': 4.816,
     'tbl_21': 4.96,
     'tbl_22': 5.052,
     'tbl_23': 5.058,
     'tbl_24': 4.701,
     'tbl_25': 4.993,
     'tbl_26': 4.906,
     'tbl_27': 4.706,
     'tbl_28': 4.801,
     'tbl_29': 4.986,
     'tbl_30': 4.305,
     'tbl_31': 4.84,
     'tbl_32': 5.011,
     'tbl_33': 4.374,
     'tbl_34': 4.546,
     'tbl_35': 4.991,
     'tbl_36': 5.071,
     'tbl_37': 4.662,
     'tbl_38': 4.751,
     'L0_rec_W2': 5.649}
    for name, (base, spread) in spreads.items():
        noise = np.random.default_rng([zlib.crc32(name.encode()), seed]).standard_normal(out[name].shape)
        drawn = base * np.exp(spread * noise) if base else spread * noise
        out[name] = jnp.asarray(drawn.astype(out[name].dtype))
    for name, factor in factors.items():
        out[name] = (out[name] * factor).astype(out[name].dtype)
    return out
```

```python
from contextlib import ExitStack

import numpy as np

import concourse.bass as bass
from concourse import mybir
from concourse.alu_op_type import AluOpType as ALU

F32 = mybir.dt.float32
BF16 = mybir.dt.bfloat16
ACT = mybir.ActivationFunctionType

B, F, D = 1024, 39, 32
K1, K2 = 128, 128
H = K1 // 2
DENSE = 16
TOP1, TOP2 = 512, 256
P = 128

TILES = B // P
Q = P // D
COLS = P // Q
PAIRS = 4
NPAIR = TILES * PAIRS
RPAIR = COLS // PAIRS
RBLK = RPAIR // 2
NB = RBLK * P
GROUPS = 3
GF = GROUPS * F
RIGHTS = 4
LAST_DIFF = F // 2
CHUNKS = 2 * (RIGHTS - 1) + 1
K_OF = [GF] * (RIGHTS - 1) + [2 * F]
GATHERS = 3
FG = F // GATHERS
QF = Q * F
GRAM = H + F
GRUN = [3, 3, 2]
QUARTERS = TILES // 2
LEAD = 2
NQ = 2 * P
M1, M2 = TOP1 // P, TOP2 // P
RING = 2 + M1 + M2 + 1


def pairs_of(p):
    i = np.arange(F)
    if p == RIGHTS - 1:
        return [(np.concatenate([i, i]), np.concatenate([i, (i + LAST_DIFF) % F]))]
    return [(np.concatenate([(i + s) % F] * GROUPS),
             np.concatenate([(i + 2 + 2 * p + 2 * (RIGHTS - 1) * g) % F for g in range(GROUPS)])) for s in range(2)]


def one_hot():
    out = np.zeros((3 * F, 2 + RIGHTS, P), np.float32)
    arrays = [pairs_of(0)[s][0] for s in range(2)] + [pairs_of(p)[0][1] for p in range(RIGHTS)]
    for n, field in enumerate(arrays):
        for part in range(3):
            out[part * F + field, n, np.arange(len(field))] = 1.0
    return out


def dlrm_tower(nc, ids, tables, one_hot_sel, identity, w1_pairs, w1_mirrored, w1_kept, w2, w_top1, b_top1,
               w_top2, b_top2, w_top3, dense_t, out):
    with ExitStack() as ctx:
        def sb(name, shape, dt=F32):
            return ctx.enter_context(nc.sbuf_tensor(name, shape, dt))

        def pb(name, shape):
            return ctx.enter_context(nc.psum_tensor(name, shape, F32))

        def sem(name):
            return ctx.enter_context(nc.semaphore(name))

        idx = sb("idx", [P, TILES, F], mybir.dt.int32)
        rows = sb("rows", [P, F, D])
        xh = sb("xh", [P, 2, COLS, GRAM])
        rest = sb("rest", [P, COLS, F])
        parts = sb("parts", [P, COLS, 3, F], BF16)
        xt = sb("xt", [3 * F, PAIRS, 2, NB], BF16)
        left = sb("left", [P, 2, 2, NB])
        prod = sb("prod", [GF, RIGHTS, 2, 2, NB])
        h1t = sb("h1t", [P, 2, NB])
        xdiag = sb("xdiag", [P, PAIRS, RPAIR, Q, F])
        gram = sb("gram", [GRAM, F, 2, Q, COLS])
        sel_raw = sb("sel_raw", [3 * F, 2 + RIGHTS, P])
        sel = sb("sel", [3 * F, 2 + RIGHTS, P], BF16)
        ident = sb("ident", [P, P])
        ident_b = sb("ident_b", [P, P], BF16)
        w1a = sb("w1a", [GF, CHUNKS, H])
        w1b = sb("w1b", [GF, CHUNKS, H])
        w1s = sb("w1s", [GF, CHUNKS, H])
        wfin = sb("wfin", [GRAM, F, K2])
        wt1a = sb("wt1a", [K2, TOP1])
        wt1b = sb("wt1b", [H + DENSE, TOP1])
        wt2 = sb("wt2", [P, M1, TOP2])
        wt3 = sb("wt3", [P, M2])
        bt1 = sb("bt1", [P, M1])
        bt2 = sb("bt2", [P, M2])
        z2 = sb("z2", [K2, NQ])
        z1 = sb("z1", [H + DENSE, QUARTERS, NQ])
        t1 = sb("t1", [P, M1, NQ])
        t2 = sb("t2", [P, M2, NQ])
        y = sb("y", [1, B])

        ps_left = pb("ps_left", [P, 2, NB])
        ps_right = pb("ps_right", [P, 2, NB])
        ps_main = pb("ps_main", [P, NB])
        ps_turn = pb("ps_turn", [P, NB])
        ps_gram = pb("ps_gram", [P, 2, NB])
        ps_turn_b = ps_turn[:].bitcast(BF16)

        ids_in = sem("ids_in")
        consts_in = sem("consts_in")
        weights_in = sem("weights_in")
        gathered = [sem(f"gathered{g}") for g in range(GATHERS)]
        out_done = sem("out_done")
        diag_zeroed = sem("diag_zeroed")
        consts_ready = sem("consts_ready")
        w1_added = sem("w1_added")
        w1_ready = sem("w1_ready")
        x_turned = sem("x_turned")
        part1_ready = sem("part1_ready")
        rest_ready = sem("rest_ready")
        part2_ready = sem("part2_ready")
        part3_ready = sem("part3_ready")
        xt_in_psum = sem("xt_in_psum")
        xt_ready = sem("xt_ready")
        diag_ready = sem("diag_ready")
        left_in_psum = sem("left_in_psum")
        left_ready = sem("left_ready")
        right_in_psum = sem("right_in_psum")
        prod_ready = sem("prod_ready")
        prod_used = sem("prod_used")
        h1t_ready = sem("h1t_ready")
        h1_turned = sem("h1_turned")
        h1_ready = sem("h1_ready")
        bank_full = sem("bank_full")
        bank_read = sem("bank_read")

        block = ctx.enter_context(nc.Block())

        def gram_use(j, k):
            return 3 * j + k + RING * (j // (2 * PAIRS))

        def tail_use(quarter, k):
            return 6 * PAIRS * (quarter + 1) + RING * quarter + k

        @block.sync
        def _(sp):
            sp.dma_start(idx[:], ids.rearrange("(t p) f -> p t f", p=P)).then_inc(ids_in, 16)
            sp.dma_start(ident[:], identity).then_inc(consts_in, 16)
            sp.dma_start(sel_raw[:], one_hot_sel).then_inc(consts_in, 16)
            sp.dma_start(w1a[:], w1_pairs).then_inc(consts_in, 16)
            sp.dma_start(w1b[:], w1_mirrored).then_inc(consts_in, 16)
            for dst, src in ((wfin[0:H], w2), (wfin[H:GRAM, :, 0:H], w1_kept),
                             (wt1a[:], w_top1[H:H + K2]), (wt1b[0:H], w_top1[0:H]),
                             (wt1b[H:H + DENSE], w_top1[H + K2:]), (wt2[:], w_top2), (wt3[:], w_top3),
                             (bt1[:], b_top1), (bt2[:], b_top2),
                             (z1[H:H + DENSE].rearrange("d a b -> d (a b)"), dense_t)):
                sp.dma_start(dst, src).then_inc(weights_in, 16)
            sp.wait_ge(bank_read, tail_use(QUARTERS - 1, RING - 1) + 1)
            sp.dma_start(out.rearrange("b o -> o b"), y[:]).then_inc(out_done, 16)
            sp.wait_ge(out_done, 16)
        WEIGHT_DMAS = 10

        @block.gpsimd
        def _(pool):
            nc.gpsimd.memset(xdiag[:], 0.0).then_inc(diag_zeroed, 1)
            pool.wait_ge(ids_in, 16)
            for t in range(TILES):
                if t >= 1:
                    pool.wait_ge(x_turned, GATHERS * t)
                for f in range(F):
                    nc.gpsimd.indirect_dma_start(
                        rows[:, f, :], None, tables[f],
                        bass.IndirectOffsetOnAxis(ap=idx[:, t, f:f + 1], axis=0)).then_inc(gathered[f // FG], 16)

        @block.vector
        def _(dve):
            dve.wait_ge(consts_in, 64)
            nc.vector.tensor_copy(ident_b[:], ident[:])
            nc.vector.tensor_copy(sel[:], sel_raw[:]).then_inc(consts_ready, 1)
            nc.vector.tensor_tensor(w1s[:], w1a[:], w1b[:], ALU.add).then_inc(w1_added, 1)
            dve.wait_ge(w1_added, 1)
            nc.vector.tensor_copy(w1s[0:F, CHUNKS - 1, :], w1a[0:F, CHUNKS - 1, :]).then_inc(w1_ready, 1)

            def turn_tile(t):
                x = xh[:, t % 2, :, H:GRAM]
                if t >= 2:
                    dve.wait_ge(bank_full, gram_use(PAIRS * (t - 1) - 1, 2) + 1)
                for g in range(GATHERS):
                    dve.wait_ge(gathered[g], 16 * FG * (t + 1))
                    nc.vector.transpose(x[:, :, g * FG:(g + 1) * FG].rearrange("p r f -> p f r"),
                                        rows[:, g * FG:(g + 1) * FG, :]).then_inc(x_turned, 1)
                dve.wait_ge(part1_ready, t + 1)
                nc.vector.tensor_tensor(rest[:], x, parts[:, :, 0, :], ALU.subtract).then_inc(rest_ready, 1)
                dve.wait_ge(part2_ready, t + 1)
                nc.vector.tensor_tensor(parts[:, :, 2, :], rest[:], parts[:, :, 1, :],
                                        ALU.subtract).then_inc(part3_ready, 1)

            def products(j, p, blk):
                n = (RIGHTS * j + p) * 2 + blk
                k = K_OF[p]
                dve.wait_ge(left_ready, 2 * j + blk + 1)
                dve.wait_ge(right_in_psum, n + 1)
                if j >= 1:
                    dve.wait_ge(prod_used, RIGHTS * (j - 1) + p + 1)
                ns = 2 if p < RIGHTS - 1 else 1
                nc.vector.tensor_tensor(prod[0:k, p, 0:ns, blk, :],
                                        ps_right[0:k, n % 2, :].unsqueeze(1).broadcast_to([k, ns, NB]),
                                        left[0:k, blk, 0:ns, :], ALU.mult).then_inc(prod_ready, 1)

            for j in range(-LEAD, NPAIR):
                if 0 <= j + LEAD < NPAIR and (j + LEAD) % PAIRS == 0:
                    turn_tile((j + LEAD) // PAIRS)
                if 0 <= j + 1 < NPAIR:
                    for p in range(RIGHTS):
                        for blk in range(2):
                            products(j + 1, p, blk)

        @block.scalar
        def _(act):
            act.wait_ge(diag_zeroed, 1)

            def split_tile(t):
                x = xh[:, t % 2, :, H:GRAM]
                act.wait_ge(x_turned, GATHERS * (t + 1))
                if t >= 1:
                    act.wait_ge(xt_in_psum, PAIRS * t)
                nc.scalar.copy(parts[:, :, 0, :], x).then_inc(part1_ready, 1)
                act.wait_ge(rest_ready, t + 1)
                nc.scalar.copy(parts[:, :, 1, :], rest[:]).then_inc(part2_ready, 1)

            def move_xt(j):
                act.wait_ge(xt_in_psum, j + 1)
                nc.scalar.copy(xt[:, j % PAIRS].rearrange("p a b -> p (a b)"),
                               ps_turn_b[0:3 * F, 0:2 * NB]).then_inc(xt_ready, 1)

            def make_diag(j):
                if j >= PAIRS:
                    act.wait_ge(bank_full, gram_use(j - PAIRS, 2) + 1)
                r0 = RPAIR * (j % PAIRS)
                for q in range(Q):
                    at = slice(q * D, (q + 1) * D)
                    done = nc.scalar.copy(xdiag[at, j % PAIRS, :, q, :],
                                          xh[at, (j // PAIRS) % 2, r0:r0 + RPAIR, H:GRAM])
                done.then_inc(diag_ready, 1)

            def move_left(j, blk):
                act.wait_ge(left_in_psum, 2 * j + blk + 1)
                if j >= 1:
                    act.wait_ge(prod_ready, (RIGHTS * (j - 1) + RIGHTS - 1) * 2 + blk + 1)
                nc.scalar.copy(left[:, blk], ps_left[:]).then_inc(left_ready, 1)

            def move_h1t(j):
                act.wait_ge(prod_used, RIGHTS * (j + 1))
                if j >= 2:
                    act.wait_ge(h1_turned, j - 1)
                nc.scalar.copy(h1t[:, j % 2, :], ps_main[:]).then_inc(h1t_ready, 1)

            def move_h1(j):
                r0 = RPAIR * (j % PAIRS)
                act.wait_ge(h1_turned, j + 1)
                if j >= 2 * PAIRS:
                    act.wait_ge(bank_full, gram_use(j - 2 * PAIRS, 2) + 1)
                dst = xh[:, (j // PAIRS) % 2, r0:r0 + RPAIR, 0:H].rearrange("p (b r) k -> p r b k", b=2)
                nc.scalar.copy(dst, ps_turn[:].rearrange("p (r b k) -> p r b k", r=RBLK, b=2)).then_inc(h1_ready, 1)

            def move_gram(j, k):
                c = gram_use(j, k)
                quarter, tile = j // (2 * PAIRS), j // PAIRS
                if quarter >= 1:
                    act.wait_ge(bank_full, tail_use(quarter - 1, 1) + 1)
                act.wait_ge(bank_full, c + 1)
                r0 = RPAIR * (j % PAIRS) + sum(GRUN[:k])
                src = ps_gram[0:GRAM, c % 2, 0:GRUN[k] * QF].rearrange("j (r q i) -> j i q r", r=GRUN[k], q=Q)
                nc.scalar.copy(gram[:, :, tile % 2, :, r0:r0 + GRUN[k]], src).then_inc(bank_read, 1)

            def move_tail(quarter):
                c = tail_use(quarter, 0)
                act.wait_ge(bank_full, c + 1)
                nc.scalar.copy(z2[:], ps_gram[:, c % 2, 0:NQ]).then_inc(bank_read, 1)
                act.wait_ge(bank_full, c + 2)
                nc.scalar.copy(z1[0:H, quarter, :], ps_gram[0:H, (c + 1) % 2, 0:NQ]).then_inc(bank_read, 1)
                for m in range(M1):
                    u = c + 2 + m
                    act.wait_ge(bank_full, u + 1)
                    nc.scalar.activation(t1[:, m, :], ps_gram[:, u % 2, 0:NQ], ACT.Relu,
                                         bias=bt1[:, m:m + 1]).then_inc(bank_read, 1)
                for m in range(M2):
                    u = c + 2 + M1 + m
                    act.wait_ge(bank_full, u + 1)
                    nc.scalar.activation(t2[:, m, :], ps_gram[:, u % 2, 0:NQ], ACT.Relu,
                                         bias=bt2[:, m:m + 1]).then_inc(bank_read, 1)
                u = c + 2 + M1 + M2
                act.wait_ge(bank_full, u + 1)
                nc.scalar.copy(y[:, quarter * NQ:(quarter + 1) * NQ], ps_gram[0:1, u % 2, 0:NQ]).then_inc(bank_read, 1)

            act.wait_ge(weights_in, 16 * WEIGHT_DMAS)
            for j in range(-LEAD, NPAIR + 3):
                gram_now = 0 <= j - 2 < NPAIR
                if 0 <= j + LEAD < NPAIR and (j + LEAD) % PAIRS == 0:
                    split_tile((j + LEAD) // PAIRS)
                if 0 <= j + 1 < NPAIR:
                    move_left(j + 1, 0)
                if 0 <= j - 1 < NPAIR:
                    make_diag(j - 1)
                    move_h1(j - 1)
                if (j - 2) % (2 * PAIRS) == 0 and j - 2 > 0:
                    move_tail((j - 2) // (2 * PAIRS) - 1)
                if 0 <= j + 1 < NPAIR:
                    move_left(j + 1, 1)
                if gram_now:
                    move_gram(j - 2, 0)
                    move_gram(j - 2, 1)
                if 0 <= j < NPAIR:
                    move_h1t(j)
                if gram_now:
                    move_gram(j - 2, 2)
                if 0 <= j + LEAD < NPAIR:
                    move_xt(j + LEAD)

        @block.tensor
        def _(pe):
            def turn_x(j):
                if j % PAIRS == 0:
                    pe.wait_ge(part3_ready, j // PAIRS + 1)
                if j >= 1:
                    pe.wait_ge(xt_ready, j)
                if j >= LEAD + 1:
                    pe.wait_ge(h1_ready, j - LEAD)
                for r in range(RPAIR):
                    last = nc.tensor.transpose(
                        ps_turn_b[0:3 * F, r * P:(r + 1) * P],
                        parts[:, RPAIR * (j % PAIRS) + r].rearrange("p a f -> p (a f)"), ident_b[:])
                last.then_inc(xt_in_psum, 1)

            def spread_left(j, blk):
                n = 2 * j + blk
                pe.wait_ge(xt_ready, j + 1)
                if n >= 1:
                    pe.wait_ge(left_ready, n)
                for s in range(2):
                    last = nc.tensor.matmul(ps_left[:, s, :], sel[:, s, :], xt[:, j % PAIRS, blk, :],
                                            start=True, stop=True)
                last.then_inc(left_in_psum, 1)

            def spread_right(j, p, blk):
                n = (RIGHTS * j + p) * 2 + blk
                if n >= 2:
                    pe.wait_ge(prod_ready, n - 1)
                nc.tensor.matmul(ps_right[:, n % 2, :], sel[:, 2 + p, :], xt[:, j % PAIRS, blk, :],
                                 start=True, stop=True).then_inc(right_in_psum, 1)

            def contract(j, p):
                if p == 0 and j >= 1:
                    pe.wait_ge(h1t_ready, j)
                pe.wait_ge(prod_ready, (RIGHTS * j + p) * 2 + 2)
                for s in range(2 if p < RIGHTS - 1 else 1):
                    c = 2 * p + s
                    for blk in range(2):
                        last = nc.tensor.matmul(ps_main[blk * H:(blk + 1) * H, :], w1s[0:K_OF[p], c, :],
                                                prod[0:K_OF[p], p, s, blk, :],
                                                start=(c == 0), stop=(c == CHUNKS - 1))
                last.then_inc(prod_used, 1)

            def turn_h1(j):
                pe.wait_ge(h1t_ready, j + 1)
                pe.wait_ge(xt_ready, min(j + LEAD + 1, NPAIR))
                if j >= 1:
                    pe.wait_ge(h1_ready, j)
                for r in range(RBLK):
                    last = nc.tensor.transpose(ps_turn[:, r * P:(r + 1) * P], h1t[:, j % 2, r * P:(r + 1) * P],
                                               ident[:])
                last.then_inc(h1_turned, 1)

            def grams(j, k):
                c = gram_use(j, k)
                if k == 0:
                    pe.wait_ge(h1_ready, j + 1)
                    pe.wait_ge(diag_ready, j + 1)
                if c >= 2:
                    pe.wait_ge(bank_read, c - 1)
                for n in range(GRUN[k]):
                    r = sum(GRUN[:k]) + n
                    last = nc.tensor.matmul(ps_gram[0:GRAM, c % 2, n * QF:(n + 1) * QF],
                                            xh[:, (j // PAIRS) % 2, RPAIR * (j % PAIRS) + r, :],
                                            xdiag[:, j % PAIRS, r].rearrange("p q i -> p (q i)"),
                                            start=True, stop=True)
                last.then_inc(bank_full, 1)

            def tail(quarter):
                c = tail_use(quarter, 0)
                pe.wait_ge(bank_read, c)
                for i in range(F):
                    g = gram[:, i].rearrange("j t q r -> j (t q r)")
                    one = nc.tensor.matmul(ps_gram[0:K2, c % 2, 0:NQ], wfin[0:H, i, :], g[0:H],
                                           start=(i == 0), stop=(i == F - 1))
                    two = nc.tensor.matmul(ps_gram[0:H, (c + 1) % 2, 0:NQ], wfin[H:GRAM, i, 0:H], g[H:GRAM],
                                           start=(i == 0), stop=(i == F - 1))
                one.then_inc(bank_full, 1)
                two.then_inc(bank_full, 1)
                pe.wait_ge(bank_read, c + 2)
                for m in range(M1):
                    u = c + 2 + m
                    pe.wait_ge(bank_read, u - 1)
                    nc.tensor.matmul(ps_gram[:, u % 2, 0:NQ], wt1a[:, m * P:(m + 1) * P], z2[:],
                                     start=True, stop=False)
                    nc.tensor.matmul(ps_gram[:, u % 2, 0:NQ], wt1b[:, m * P:(m + 1) * P], z1[:, quarter, :],
                                     start=False, stop=True).then_inc(bank_full, 1)
                pe.wait_ge(bank_read, c + 2 + M1)
                for m in range(M2):
                    u = c + 2 + M1 + m
                    for k in range(M1):
                        last = nc.tensor.matmul(ps_gram[:, u % 2, 0:NQ], wt2[:, k, m * P:(m + 1) * P], t1[:, k, :],
                                                start=(k == 0), stop=(k == M1 - 1))
                    last.then_inc(bank_full, 1)
                u = c + 2 + M1 + M2
                pe.wait_ge(bank_read, u)
                for k in range(M2):
                    last = nc.tensor.matmul(ps_gram[0:1, u % 2, 0:NQ], wt3[:, k:k + 1], t2[:, k, :],
                                            start=(k == 0), stop=(k == M2 - 1))
                last.then_inc(bank_full, 1)

            pe.wait_ge(consts_ready, 1)
            pe.wait_ge(w1_ready, 1)
            pe.wait_ge(weights_in, 16 * WEIGHT_DMAS)
            for j in range(-LEAD, NPAIR + 3):
                feed = 0 <= j + 1 < NPAIR
                main = 0 <= j < NPAIR
                gram_now = 0 <= j - 2 < NPAIR
                if feed:
                    spread_left(j + 1, 0)
                if main:
                    contract(j, 0)
                if 0 <= j - 1 < NPAIR:
                    turn_h1(j - 1)
                if (j - 2) % (2 * PAIRS) == 0 and j - 2 > 0:
                    tail((j - 2) // (2 * PAIRS) - 1)
                if feed:
                    spread_right(j + 1, 0, 0)
                    spread_left(j + 1, 1)
                    spread_right(j + 1, 0, 1)
                for p in range(1, RIGHTS):
                    if main:
                        contract(j, p)
                    if feed:
                        spread_right(j + 1, p, 0)
                        spread_right(j + 1, p, 1)
                    if gram_now:
                        grams(j - 2, p - 1)
                if 0 <= j + LEAD < NPAIR:
                    turn_x(j + LEAD)


def kernel(**inputs):
    from concourse import bacc
    from concourse.bass_utils import run_bass_kernel_spmd

    nc = bacc.Bacc("TRN2", target_bir_lowering=False, num_devices=1)
    arrays = {}

    def give(name, a):
        a = np.ascontiguousarray(a)
        arrays[name] = a
        return nc.dram_tensor(name, a.shape, mybir.dt.from_np(a.dtype), kind="ExternalInput").ap()

    ids = give("ids", np.asarray(inputs["ids"]))
    tables = [give(f"tbl_{f}", np.asarray(inputs[f"tbl_{f}"])) for f in range(F)]
    w1 = np.asarray(inputs["L0_rec_W1"]).reshape(F, F, K1)
    forward = np.zeros((GF, CHUNKS, H), w1.dtype)
    mirrored = np.zeros((GF, CHUNKS, H), w1.dtype)
    for p in range(RIGHTS):
        for s, (i, j) in enumerate(pairs_of(p)):
            forward[0:K_OF[p], 2 * p + s] = w1[i, j, 0:H]
            mirrored[0:K_OF[p], 2 * p + s] = w1[j, i, 0:H]
    w2 = np.asarray(inputs["L0_rec_W2"]).reshape(F, H, K2)
    out = nc.dram_tensor("out", (B, 1), F32, kind="ExternalOutput").ap()
    dlrm_tower(
        nc, ids, tables, give("one_hot", one_hot()), give("identity", np.eye(P, dtype=np.float32)),
        give("w1_pairs", forward), give("w1_mirrored", mirrored),
        give("w1_kept", w1[:, :, H:].transpose(1, 0, 2)), give("w2", w2.transpose(1, 0, 2)),
        give("w_top1", np.asarray(inputs["W_top1"])),
        give("b_top1", np.asarray(inputs["b_top1"]).reshape(M1, P).T),
        give("w_top2", np.asarray(inputs["W_top2"]).reshape(M1, P, TOP2).transpose(1, 0, 2)),
        give("b_top2", np.asarray(inputs["b_top2"]).reshape(M2, P).T),
        give("w_top3", np.asarray(inputs["W_top3"]).reshape(M2, P).T),
        give("dense_t", np.asarray(inputs["dense_ctx"]).T), out)
    return run_bass_kernel_spmd(nc, [arrays], core_ids=[0]).results[0]["out"]
```

```python
from contextlib import ExitStack

import numpy as np

import concourse.bass as bass
from concourse import mybir
from concourse.alu_op_type import AluOpType as ALU

F32 = mybir.dt.float32
BF16 = mybir.dt.bfloat16
ACT = mybir.ActivationFunctionType

B, F, D = 1024, 39, 32
K1, K2 = 128, 128
H = K1 // 2
DENSE = 16
TOP1, TOP2 = 512, 256
P = 128

Q = P // D
RPAIR = 8
NPAIR = B // (Q * RPAIR)
A = P // (Q * RPAIR)
GATHERS = -(-F // A)
FPAD = GATHERS * A
ROW_SLOTS = 6
XH_SLOTS = 8
RBLK = RPAIR // 2
NB = RBLK * P
GROUPS = 3
GF = GROUPS * F
SHIFTS = [4, 3]
RIGHTS = len(SHIFTS)
LEFTS = max(SHIFTS)
CHUNKS = sum(SHIFTS)
SHIFT_ROWS = 120
QF = Q * F
GRAM = H + F
GRUN = [3, 3, 2]
QUARTERS = 4
QPAIRS = NPAIR // QUARTERS
NQ = B // QUARTERS
I2 = -(-F // 2)
GATHER_BOUND = 8
LEAD = 2
M1, M2 = TOP1 // P, TOP2 // P


def pair_fields(p, s):
    g, i = np.divmod(np.arange(GF), F)
    return (i + s) % F, (i + CHUNKS * g + sum(SHIFTS[:p + 1]) - 1) % F


def one_hot():
    out = np.zeros((3 * F, 1 + RIGHTS, P), np.float32)
    arrays = [np.arange(P) % F] + [pair_fields(p, 0)[1] for p in range(RIGHTS)]
    for n, field in enumerate(arrays):
        for part in range(3):
            out[part * F + field, n, np.arange(len(field))] = 1.0
    return out


def dlrm_tower(nc, ids, starts, table, one_hot_sel, identity, w1_pairs, w1_mirrored, w1_kept, w2, w_top1, b_top1,
               w_top2, b_top2, w_top3, dense_t, out):
    with ExitStack() as ctx:
        def sb(name, shape, dt=F32):
            return ctx.enter_context(nc.sbuf_tensor(name, shape, dt))

        def pb(name, shape):
            return ctx.enter_context(nc.psum_tensor(name, shape, F32))

        def sem(name):
            return ctx.enter_context(nc.semaphore(name))

        ids_raw = sb("ids_raw", [P, NPAIR, GATHERS], mybir.dt.int32)
        field_start = sb("field_start", [P, GATHERS], mybir.dt.int32)
        idx = sb("idx", [P, NPAIR, GATHERS], mybir.dt.int32)
        rows = sb("rows", [P, ROW_SLOTS, GATHERS, D])
        xh = sb("xh", [P, XH_SLOTS, RPAIR, H + FPAD])
        rest = sb("rest", [P, RPAIR, F])
        parts = sb("parts", [P, 2, RPAIR, 3, F], BF16)
        xt = sb("xt", [3 * F, 2, 2, NB], BF16)
        left = sb("left", [P, 2, LEFTS, 2, NB])
        prod = sb("prod", [GF, CHUNKS, 2, NB])
        h1t = sb("h1t", [P, 2, NB])
        xdiag = sb("xdiag", [P, 2, RPAIR, Q, F])
        gh = sb("gh", [P, I2, QPAIRS, Q, RPAIR])
        gx = sb("gx", [H + F, I2, QPAIRS, Q, RPAIR])
        sel = sb("sel", [3 * F, 1 + RIGHTS, P], BF16)
        ident = sb("ident", [P, P])
        ident_b = sb("ident_b", [P, P], BF16)
        w1s = sb("w1s", [GF, CHUNKS, H])
        w2s = sb("w2s", [P, I2, K2])
        w1k = sb("w1k", [H + F, I2, K1 - H])
        wt1a = sb("wt1a", [K2, TOP1])
        wt1b = sb("wt1b", [H + DENSE, TOP1])
        wt2 = sb("wt2", [P, M1, TOP2])
        wt3 = sb("wt3", [P, M2])
        bt1 = sb("bt1", [P, M1])
        bt2 = sb("bt2", [P, M2])
        z2 = sb("z2", [K2, NQ])
        z1 = sb("z1", [H + DENSE, QUARTERS, NQ])
        t1 = sb("t1", [P, M1, NQ])
        t2 = sb("t2", [P, M2, NQ])
        y = sb("y", [1, NQ])
        stage = gh[:].rearrange("p i j q r -> p (i j q r)")
        sel_raw = stage[0:3 * F, 0:(1 + RIGHTS) * P].rearrange("p (n m) -> p n m", m=P)
        w1a = stage[0:GF, NB:NB + CHUNKS * H].rearrange("p (c k) -> p c k", k=H)
        w1b = stage[0:GF, 2 * NB:2 * NB + CHUNKS * H].rearrange("p (c k) -> p c k", k=H)

        ps_left = pb("ps_left", [P, 2, NB])
        ps_right = pb("ps_right", [P, 2, NB])
        ps_main = pb("ps_main", [P, NB])
        ps_turn = pb("ps_turn", [P, NB])
        ps_gram = pb("ps_gram", [P, 2, NB])
        ps_turn_b = ps_turn[:].bitcast(BF16)

        ids_in = sem("ids_in")
        consts_in = sem("consts_in")
        weights_in = sem("weights_in")
        idx_ready = sem("idx_ready")
        gathered = [sem(f"gathered{n}") for n in range(ROW_SLOTS)]
        out_done = sem("out_done")
        diag_zeroed = sem("diag_zeroed")
        sel_ready = sem("sel_ready")
        ident_ready = sem("ident_ready")
        w1_added = sem("w1_added")
        w1_ready = sem("w1_ready")
        gx_zeroed = sem("gx_zeroed")
        x_turned = sem("x_turned")
        part1_ready = sem("part1_ready")
        rest_ready = sem("rest_ready")
        part2_ready = sem("part2_ready")
        part3_ready = sem("part3_ready")
        xt_in_psum = sem("xt_in_psum")
        xt_ready = sem("xt_ready")
        diag_ready = sem("diag_ready")
        left_in_psum = sem("left_in_psum")
        left_ready = sem("left_ready")
        shifted = [sem(f"shifted{n}") for n in range(2)]
        right_in_psum = sem("right_in_psum")
        prod_ready = sem("prod_ready")
        prod_used = sem("prod_used")
        h1t_ready = sem("h1t_ready")
        h1_turned = sem("h1_turned")
        h1_ready = sem("h1_ready")
        bank_full = sem("bank_full")
        bank_read = sem("bank_read")

        block = ctx.enter_context(nc.Block())

        order = []
        for j in range(NPAIR + 1):
            here = [("gram", j, k) for k in range(len(GRUN))] if j < NPAIR else []
            if j and j % QPAIRS == 0:
                quarter = j // QPAIRS - 1
                stages = [[("sum2", quarter), ("sum1", quarter)], [("top1", quarter, m) for m in range(M1)],
                          [("top2", quarter, m) for m in range(M2)], [("top3", quarter)]]
                here = sum((stages[n] + here[n:n + 1] for n in range(len(stages))), [])
            order += here
        use = {what: n for n, what in enumerate(order)}

        weights = [(w2s[:], w2), (w1k[:], w1_kept),
                   (wt1a[:], w_top1[H:H + K2]), (wt1b[0:H], w_top1[0:H]), (wt1b[H:H + DENSE], w_top1[H + K2:]),
                   (wt2[:], w_top2), (wt3[:], w_top3), (bt1[:], b_top1), (bt2[:], b_top2),
                   (z1[H:H + DENSE].rearrange("d a b -> d (a b)"), dense_t)]

        @block.sync
        def _(sp):
            sp.dma_start(ids_raw[:], ids).then_inc(ids_in, 16)
            sp.dma_start(field_start[:], starts).then_inc(ids_in, 16)
            for dst, src in ((ident[:], identity), (sel_raw, one_hot_sel), (w1a, w1_pairs), (w1b, w1_mirrored)):
                sp.dma_start(dst, src).then_inc(consts_in, 16)
            for dst, src in weights:
                sp.dma_start(dst, src).then_inc(weights_in, 16)
            for j in range(NPAIR):
                sp.wait_ge(left_ready, j + 1)
                if j >= 2:
                    sp.wait_ge(prod_ready, 2 * RIGHTS * (j - 1))
                for s in range(1, LEFTS):
                    sp.dma_start(left[0:SHIFT_ROWS, j % 2, s], left[s:s + SHIFT_ROWS, j % 2, 0])\
                      .then_inc(shifted[j % 2], 16)

        @block.gpsimd
        def _(pool):
            pool.wait_ge(idx_ready, 1)
            for j in range(NPAIR):
                slot = j % ROW_SLOTS
                if j >= ROW_SLOTS:
                    pool.wait_ge(x_turned, j - ROW_SLOTS + 1)
                for g in range(GATHERS):
                    nc.gpsimd.indirect_dma_start(
                        rows[:, slot, g, :], None, table,
                        bass.IndirectOffsetOnAxis(ap=idx[:, j, g:g + 1], axis=0)).then_inc(gathered[slot], 16)

        @block.vector
        def _(dve):
            dve.wait_ge(ids_in, 32)
            nc.vector.tensor_tensor(idx[:], ids_raw[:], field_start[:].unsqueeze(1).broadcast_to([P, NPAIR, GATHERS]),
                                    ALU.add).then_inc(idx_ready, 1)
            nc.vector.memset(xdiag[:], 0.0).then_inc(diag_zeroed, 1)
            nc.vector.memset(gx[D:H], 0.0).then_inc(gx_zeroed, 1)
            dve.wait_ge(consts_in, 64)
            nc.vector.tensor_copy(ident_b[:], ident[:]).then_inc(ident_ready, 1)
            nc.vector.tensor_copy(sel[:], sel_raw).then_inc(sel_ready, 1)
            nc.vector.tensor_tensor(w1s[:], w1a, w1b, ALU.add).then_inc(w1_added, 1)
            dve.wait_ge(w1_added, 1)
            nc.vector.tensor_copy(w1s[0:F, SHIFTS[0] - 1, :], w1a[0:F, SHIFTS[0] - 1, :]).then_inc(w1_ready, 1)

            def turn_pair(j):
                slot = j % ROW_SLOTS
                dve.wait_ge(gathered[slot], 16 * GATHERS * (j // ROW_SLOTS + 1))
                if j >= XH_SLOTS:
                    dve.wait_ge(bank_full, use["gram", j - XH_SLOTS, 2] + 1)
                nc.vector.transpose(xh[:, j % XH_SLOTS, :, H:].rearrange("p r (g a) -> p g r a", a=A),
                                    rows[:, slot].rearrange("p g (r a) -> p g r a", a=A)).then_inc(x_turned, 1)

            def split_pair(j):
                x = xh[:, j % XH_SLOTS, :, H:GRAM]
                if j >= 2:
                    dve.wait_ge(xt_in_psum, j - 1)
                dve.wait_ge(x_turned, j + 1)
                nc.vector.tensor_copy(parts[:, j % 2, :, 0, :], x).then_inc(part1_ready, 1)
                dve.wait_ge(part1_ready, j + 1)
                nc.vector.tensor_tensor(rest[:], x, parts[:, j % 2, :, 0, :], ALU.subtract).then_inc(rest_ready, 1)
                dve.wait_ge(rest_ready, j + 1)
                nc.vector.tensor_copy(parts[:, j % 2, :, 1, :], rest[:]).then_inc(part2_ready, 1)
                dve.wait_ge(part2_ready, j + 1)
                nc.vector.tensor_tensor(parts[:, j % 2, :, 2, :], rest[:], parts[:, j % 2, :, 1, :],
                                        ALU.subtract).then_inc(part3_ready, 1)

            def products(j, p, blk):
                n = (RIGHTS * j + p) * 2 + blk
                c = sum(SHIFTS[:p])
                ns = SHIFTS[p]
                if p == 0 and blk == 0:
                    dve.wait_ge(left_ready, j + 1)
                    dve.wait_ge(shifted[j % 2], 16 * (LEFTS - 1) * (j // 2 + 1))
                dve.wait_ge(right_in_psum, n + 1)
                if j >= 1:
                    dve.wait_ge(prod_used, RIGHTS * (j - 1) + p + 1)
                nc.vector.tensor_tensor(prod[:, c:c + ns, blk, :],
                                        ps_right[0:GF, n % 2, :].unsqueeze(1).broadcast_to([GF, ns, NB]),
                                        left[0:GF, j % 2, 0:ns, blk, :], ALU.mult).then_inc(prod_ready, 1)

            for j in range(-LEAD, NPAIR):
                if j + LEAD < GATHER_BOUND:
                    turn_pair(j + LEAD)
                    split_pair(j + LEAD)
                for p in range(RIGHTS):
                    if p == 1 and GATHER_BOUND <= j + LEAD + 1 < NPAIR:
                        turn_pair(j + LEAD + 1)
                        split_pair(j + LEAD + 1)
                    if 0 <= j + 1 < NPAIR:
                        for blk in range(2):
                            products(j + 1, p, blk)

        @block.scalar
        def _(act):
            act.wait_ge(diag_zeroed, 1)

            def move_xt(j):
                act.wait_ge(xt_in_psum, j + 1)
                nc.scalar.copy(xt[:, j % 2].rearrange("p a b -> p (a b)"),
                               ps_turn_b[0:3 * F, 0:2 * NB]).then_inc(xt_ready, 1)

            def make_diag(j):
                if j >= 2:
                    act.wait_ge(bank_full, use["gram", j - 2, 2] + 1)
                act.wait_ge(x_turned, j + 1)
                for q in range(Q):
                    at = slice(q * D, (q + 1) * D)
                    done = nc.scalar.copy(xdiag[at, j % 2, :, q, :],
                                          xh[at, j % XH_SLOTS, :, H:GRAM])
                done.then_inc(diag_ready, 1)

            def move_left(j):
                act.wait_ge(left_in_psum, j + 1)
                if j >= 2:
                    act.wait_ge(prod_ready, 2 * RIGHTS * (j - 1))
                    act.wait_ge(shifted[j % 2], 16 * (LEFTS - 1) * (j // 2))
                nc.scalar.copy(left[:, j % 2, 0], ps_left[:]).then_inc(left_ready, 1)

            def move_h1t(j):
                act.wait_ge(prod_used, RIGHTS * (j + 1))
                if j >= 2:
                    act.wait_ge(h1_turned, j - 1)
                nc.scalar.copy(h1t[:, j % 2, :], ps_main[:]).then_inc(h1t_ready, 1)

            def move_h1(j):
                act.wait_ge(h1_turned, j + 1)
                if j >= XH_SLOTS:
                    act.wait_ge(bank_full, use["gram", j - XH_SLOTS, 2] + 1)
                dst = xh[:, j % XH_SLOTS, :, 0:H].rearrange("p (b r) k -> p r b k", b=2)
                nc.scalar.copy(dst, ps_turn[:].rearrange("p (r b k) -> p r b k", r=RBLK, b=2)).then_inc(h1_ready, 1)

            def move_gram(j, k):
                c = use["gram", j, k]
                quarter = j // QPAIRS
                if quarter == 0:
                    act.wait_ge(w1_ready, 1)
                    act.wait_ge(gx_zeroed, 1)
                else:
                    act.wait_ge(bank_full, use["sum1", quarter - 1] + 1)
                act.wait_ge(bank_full, c + 1)
                r = slice(sum(GRUN[:k]), sum(GRUN[:k + 1]))
                src = ps_gram[:, c % 2, 0:GRUN[k] * QF].rearrange("j (r q i) -> j i q r", r=GRUN[k], q=Q)
                for odd in range(2):
                    n = len(range(odd, F, 2))
                    nc.scalar.copy(gh[odd * H:(odd + 1) * H, 0:n, j % QPAIRS, :, r], src[0:H, odd::2])
                    last = nc.scalar.copy(gx[odd * H:odd * H + F, 0:n, j % QPAIRS, :, r], src[H:GRAM, odd::2])
                last.then_inc(bank_read, 1)

            def move_sums(quarter):
                c = use["sum2", quarter]
                act.wait_ge(bank_full, c + 1)
                nc.scalar.copy(z2[:], ps_gram[:, c % 2, 0:NQ]).then_inc(bank_read, 1)
                act.wait_ge(bank_full, c + 2)
                for half in range(2):
                    last = nc.scalar.copy(z1[0:K1 - H, quarter, half * P:(half + 1) * P],
                                          ps_gram[half * H:(half + 1) * H, (c + 1) % 2, 0:P])
                last.then_inc(bank_read, 1)

            def move_top(stage, quarter, count, dst, bias):
                for m in range(count):
                    c = use[stage, quarter, m]
                    act.wait_ge(bank_full, c + 1)
                    nc.scalar.activation(dst[:, m, :], ps_gram[:, c % 2, 0:NQ], ACT.Relu,
                                         bias=bias[:, m:m + 1]).then_inc(bank_read, 1)

            def give_y(quarter):
                c = use["top3", quarter]
                act.wait_ge(bank_full, c + 1)
                if quarter >= 1:
                    act.wait_ge(out_done, 16 * quarter)
                nc.scalar.copy(y[:], ps_gram[0:1, c % 2, 0:NQ]).then_inc(bank_read, 1)
                act.wait_ge(bank_read, c + 1)
                act.dma_start(out[quarter * NQ:(quarter + 1) * NQ, :].rearrange("b o -> o b"), y[:])\
                   .then_inc(out_done, 16)

            act.wait_ge(weights_in, 16 * len(weights))
            for j in range(-LEAD, NPAIR + 2):
                gram_now = 0 <= j - 1 < NPAIR
                tail_now = (j - 1) % QPAIRS == 0 and j - 1 > 0
                quarter = (j - 1) // QPAIRS - 1
                if gram_now:
                    move_h1(j - 1)
                if j + LEAD < NPAIR:
                    move_xt(j + LEAD)
                if tail_now:
                    move_sums(quarter)
                if gram_now:
                    move_gram(j - 1, 0)
                if j + LEAD < NPAIR:
                    move_left(j + LEAD)
                if tail_now:
                    move_top("top1", quarter, M1, t1, bt1)
                if gram_now:
                    move_gram(j - 1, 1)
                if tail_now:
                    move_top("top2", quarter, M2, t2, bt2)
                if 0 <= j < NPAIR:
                    move_h1t(j)
                if gram_now:
                    move_gram(j - 1, 2)
                if tail_now:
                    give_y(quarter)
                if 0 <= j < NPAIR:
                    make_diag(j)
            act.wait_ge(out_done, 16 * QUARTERS)

        @block.tensor
        def _(pe):
            def turn_x(j):
                pe.wait_ge(part3_ready, j + 1)
                if j >= 1:
                    pe.wait_ge(xt_ready, j)
                if j >= LEAD + 1:
                    pe.wait_ge(h1_ready, j - LEAD)
                for r in range(RPAIR):
                    last = nc.tensor.transpose(ps_turn_b[0:3 * F, r * P:(r + 1) * P],
                                               parts[:, j % 2, r].rearrange("p a f -> p (a f)"), ident_b[:])
                last.then_inc(xt_in_psum, 1)

            def spread_left(j):
                pe.wait_ge(xt_ready, j + 1)
                if j >= 1:
                    pe.wait_ge(left_ready, j)
                for blk in range(2):
                    last = nc.tensor.matmul(ps_left[:, blk, :], sel[:, 0, :], xt[:, j % 2, blk, :],
                                            start=True, stop=True)
                last.then_inc(left_in_psum, 1)

            def spread_right(j, p, blk):
                n = (RIGHTS * j + p) * 2 + blk
                if n >= 2:
                    pe.wait_ge(prod_ready, n - 1)
                nc.tensor.matmul(ps_right[:, n % 2, :], sel[:, 1 + p, :], xt[:, j % 2, blk, :],
                                 start=True, stop=True).then_inc(right_in_psum, 1)

            def contract(j, p):
                if p == 0 and j >= 1:
                    pe.wait_ge(h1t_ready, j)
                pe.wait_ge(prod_ready, (RIGHTS * j + p) * 2 + 2)
                for c in range(sum(SHIFTS[:p]), sum(SHIFTS[:p + 1])):
                    for blk in range(2):
                        last = nc.tensor.matmul(ps_main[blk * H:(blk + 1) * H, :], w1s[:, c, :], prod[:, c, blk, :],
                                                start=(c == 0), stop=(c == CHUNKS - 1))
                last.then_inc(prod_used, 1)

            def turn_h1(j):
                pe.wait_ge(h1t_ready, j + 1)
                pe.wait_ge(xt_ready, min(j + LEAD + 1, NPAIR))
                if j >= 1:
                    pe.wait_ge(h1_ready, j)
                for r in range(RBLK):
                    last = nc.tensor.transpose(ps_turn[:, r * P:(r + 1) * P], h1t[:, j % 2, r * P:(r + 1) * P],
                                               ident[:])
                last.then_inc(h1_turned, 1)

            def grams(j, k):
                c = use["gram", j, k]
                if k == 0:
                    pe.wait_ge(h1_ready, j + 1)
                    pe.wait_ge(diag_ready, j + 1)
                if c >= 2:
                    pe.wait_ge(bank_read, c - 1)
                for n in range(GRUN[k]):
                    r = sum(GRUN[:k]) + n
                    last = nc.tensor.matmul(ps_gram[0:GRAM, c % 2, n * QF:(n + 1) * QF],
                                            xh[:, j % XH_SLOTS, r, 0:GRAM],
                                            xdiag[:, j % 2, r].rearrange("p q i -> p (q i)"),
                                            start=True, stop=True)
                last.then_inc(bank_full, 1)

            def sums(quarter):
                c = use["sum2", quarter]
                pe.wait_ge(bank_read, c)
                for n in range(I2):
                    of = slice(0, P if 2 * n + 1 < F else H)
                    last = nc.tensor.matmul(ps_gram[:, c % 2, 0:NQ], w2s[of, n, :],
                                            gh[of, n].rearrange("k j q r -> k (j q r)"),
                                            start=(n == 0), stop=(n == I2 - 1))
                last.then_inc(bank_full, 1)
                for n in range(I2):
                    of = slice(0, H + F if 2 * n + 1 < F else F)
                    for half in range(2):
                        last = nc.tensor.matmul(ps_gram[half * H:(half + 1) * H, (c + 1) % 2, 0:P], w1k[of, n, :],
                                                gx[of, n, half * QPAIRS // 2:(half + 1) * QPAIRS // 2]
                                                .rearrange("k j q r -> k (j q r)"),
                                                start=(n == 0), stop=(n == I2 - 1))
                last.then_inc(bank_full, 1)

            def top(stage, quarter, m, operands):
                c = use[stage, quarter, m] if m is not None else use[stage, quarter]
                pe.wait_ge(bank_read, c - 1)
                rows_out = P if m is not None else 1
                for n, (w, x) in enumerate(operands):
                    last = nc.tensor.matmul(ps_gram[0:rows_out, c % 2, 0:NQ], w, x,
                                            start=(n == 0), stop=(n == len(operands) - 1))
                last.then_inc(bank_full, 1)

            def top1(quarter):
                pe.wait_ge(bank_read, use["sum1", quarter] + 1)
                for m in range(M1):
                    at = slice(m * P, (m + 1) * P)
                    top("top1", quarter, m, [(wt1a[:, at], z2[:]), (wt1b[:, at], z1[:, quarter, :])])

            def top2(quarter):
                pe.wait_ge(bank_read, use["top1", quarter, M1 - 1] + 1)
                for m in range(M2):
                    top("top2", quarter, m, [(wt2[:, k, m * P:(m + 1) * P], t1[:, k, :]) for k in range(M1)])

            def top3(quarter):
                pe.wait_ge(bank_read, use["top2", quarter, M2 - 1] + 1)
                top("top3", quarter, None, [(wt3[:, k:k + 1], t2[:, k, :]) for k in range(M2)])

            pe.wait_ge(ident_ready, 1)
            pe.wait_ge(sel_ready, 1)
            pe.wait_ge(w1_ready, 1)
            pe.wait_ge(weights_in, 16 * len(weights))
            for j in range(-LEAD, NPAIR + 2):
                feed = 0 <= j + 1 < NPAIR
                main = 0 <= j < NPAIR
                gram_now = 0 <= j - 1 < NPAIR
                tail_now = (j - 1) % QPAIRS == 0 and j - 1 > 0
                quarter = (j - 1) // QPAIRS - 1
                if gram_now:
                    turn_h1(j - 1)
                if main:
                    contract(j, 0)
                if feed:
                    spread_right(j + 1, 0, 0)
                    spread_right(j + 1, 0, 1)
                if j + LEAD < NPAIR:
                    turn_x(j + LEAD)
                if tail_now:
                    sums(quarter)
                if gram_now:
                    grams(j - 1, 0)
                if j + LEAD < NPAIR:
                    spread_left(j + LEAD)
                if tail_now:
                    top1(quarter)
                if gram_now:
                    grams(j - 1, 1)
                if tail_now:
                    top2(quarter)
                if main:
                    contract(j, 1)
                if feed:
                    spread_right(j + 1, 1, 0)
                    spread_right(j + 1, 1, 1)
                if gram_now:
                    grams(j - 1, 2)
                if tail_now:
                    top3(quarter)


def kernel(**inputs):
    from concourse import bacc
    from concourse.bass_utils import run_bass_kernel_spmd

    nc = bacc.Bacc("TRN2", target_bir_lowering=False, num_devices=1)
    arrays = {}

    def give(name, a):
        a = np.ascontiguousarray(a)
        arrays[name] = a
        return nc.dram_tensor(name, a.shape, mybir.dt.from_np(a.dtype), kind="ExternalInput").ap()

    tables = [np.asarray(inputs[f"tbl_{f}"]) for f in range(F)]
    fields = np.minimum(np.arange(FPAD), F - 1)
    ids = np.asarray(inputs["ids"])[:, fields].reshape(NPAIR, Q, RPAIR, GATHERS, A)
    ids = ids.transpose(1, 2, 4, 0, 3).reshape(P, NPAIR, GATHERS)
    start = np.concatenate([[0], np.cumsum([len(t) for t in tables])]).astype(np.int32)[fields]
    start = np.tile(start.reshape(GATHERS, A).T, (Q * RPAIR, 1))
    w1 = np.asarray(inputs["L0_rec_W1"]).reshape(F, F, K1)
    forward = np.zeros((GF, CHUNKS, H), w1.dtype)
    mirrored = np.zeros((GF, CHUNKS, H), w1.dtype)
    for p in range(RIGHTS):
        for s in range(SHIFTS[p]):
            i, j = pair_fields(p, s)
            c = sum(SHIFTS[:p]) + s
            forward[:, c], mirrored[:, c] = w1[i, j, 0:H], w1[j, i, 0:H]
    forward[(GROUPS - 1) * F:, sum(SHIFTS[:RIGHTS - 1])] = 0
    mirrored[(GROUPS - 1) * F:, sum(SHIFTS[:RIGHTS - 1])] = 0
    w2 = np.asarray(inputs["L0_rec_W2"]).reshape(F, H, K2)
    w2_rows = np.zeros((P, I2, K2), w2.dtype)
    kept_rows = np.zeros((H + F, I2, K1 - H), w1.dtype)
    for odd in range(2):
        n = len(range(odd, F, 2))
        w2_rows[odd * H:(odd + 1) * H, :n] = w2[odd::2].transpose(1, 0, 2)
        kept_rows[odd * H:odd * H + F, :n] = w1[odd::2, :, H:].transpose(1, 0, 2)
    out = nc.dram_tensor("out", (B, 1), F32, kind="ExternalOutput").ap()
    dlrm_tower(
        nc, give("ids", ids), give("starts", start), give("table", np.concatenate(tables)), give("one_hot", one_hot()), give("identity", np.eye(P, dtype=np.float32)),
        give("w1_pairs", forward), give("w1_mirrored", mirrored),
        give("w1_kept", kept_rows), give("w2", w2_rows),
        give("w_top1", np.asarray(inputs["W_top1"])),
        give("b_top1", np.asarray(inputs["b_top1"]).reshape(M1, P).T),
        give("w_top2", np.asarray(inputs["W_top2"]).reshape(M1, P, TOP2).transpose(1, 0, 2)),
        give("b_top2", np.asarray(inputs["b_top2"]).reshape(M2, P).T),
        give("w_top3", np.asarray(inputs["W_top3"]).reshape(M2, P).T),
        give("dense_t", np.asarray(inputs["dense_ctx"]).T), out)
    return run_bass_kernel_spmd(nc, [arrays], core_ids=[0]).results[0]["out"]
```
